# Optimizing a Trainium2 kernel written in Bass

```python
import numpy as np
import jax
import jax.numpy as jnp

def _softmax(x, axis=-1):
    return jax.nn.softmax(x, axis=axis)
def _gelu(x):
    return jax.nn.gelu(x, approximate=True)
def _silu(x):
    return jax.nn.silu(x)
def _sigmoid(x):
    return jax.nn.sigmoid(x)
def _layernorm(x, axis=-1, eps=1e-5):
    m = jnp.mean(x, axis=axis, keepdims=True)
    v = jnp.var(x, axis=axis, keepdims=True)
    return (x - m) / jnp.sqrt(v + eps)
def _scatter_add(tgt, idx, src, axis=0):
    return tgt.at[idx].add(src)
def _segment_sum(src, seg, n):
    return jax.ops.segment_sum(src, seg, n)

kernel_name = 'mk_conv_preact_d1_conv_nchw384_946706'

def setup_inputs(seed: int = 0):
    np.random.seed(seed)
    _w = jnp.asarray
    def _rec_inputs():
        import jax
        import jax.numpy as jnp
        _gk = jax.random.key(seed)
        x = -4.65e-05 + 0.9999 * jax.random.normal(jax.random.fold_in(_gk, 1), (32, 384, 64, 64), jnp.float32)
        return x
    x = _rec_inputs()
    def _L0_conv_setup():
        import jax, jax.numpy as jnp
        from jax import lax
        import numpy as np
        H, W = (64, 64)
        K = 5
        SIGMA = 0.5
        CHAN_PER_POS = 8
        INIT_STRIDE = 16
        BATCH = 32

        def _num_offsets(h, w, s):
            ny = (h - s) // s * 2 + 1
            nx = (w - s) // s * 2 + 1
            return (ny, nx, ny * nx - 1)

        def _displace(x, off_int):
            _, _, _, h, w = x.shape

            def shift_one(xp, dxy):
                dx, dy = (dxy[0], dxy[1])
                ys = jnp.arange(h) - dy
                xs = jnp.arange(w) - dx
                ym = (ys >= 0) & (ys < h)
                xm = (xs >= 0) & (xs < w)
                ysc = jnp.clip(ys, 0, h - 1)
                xsc = jnp.clip(xs, 0, w - 1)
                out = xp[:, :, ysc][:, :, :, xsc]
                return out * (ym[:, None] & xm[None, :]).astype(xp.dtype)
            return jax.vmap(shift_one, in_axes=(1, 0), out_axes=1)(x, off_int)
        key = jax.random.key(seed)
        k1, k2 = jax.random.split(key)
        ny, nx, npos = _num_offsets(H, W, INIT_STRIDE)
        C = npos * CHAN_PER_POS
        x = jax.random.normal(k1, (BATCH, C, H, W), dtype=jnp.float32)
        offs = []
        for ih in range(-(ny // 2), ny // 2 + 1):
            for iw in range(-(nx // 2), nx // 2 + 1):
                if ih == 0 and iw == 0:
                    continue
                offs.append([iw * INIT_STRIDE, ih * INIT_STRIDE])
        offset = jnp.asarray(np.array(offs, dtype=np.float32))
        offset = offset + jax.random.uniform(k2, offset.shape, dtype=jnp.float32, minval=-0.4, maxval=0.4)
        return {'x': x, 'offset': offset}
    _L0_conv_all = _L0_conv_setup()
    _L0_conv_in = {k: v for k, v in _L0_conv_all.items() if k in ('offset', )}
    del _L0_conv_all

    return {
        "x": x,
        "L0_conv_offset": _L0_conv_in["offset"],
    }

def reference(x, L0_conv_offset):
    import jax
    import jax.numpy as jnp
    def _L0_conv_ref(x, offset):
        import jax, jax.numpy as jnp
        from jax import lax
        import numpy as np
        H, W = (64, 64)
        K = 5
        SIGMA = 0.5
        CHAN_PER_POS = 8
        INIT_STRIDE = 16
        BATCH = 32

        def _num_offsets(h, w, s):
            ny = (h - s) // s * 2 + 1
            nx = (w - s) // s * 2 + 1
            return (ny, nx, ny * nx - 1)

        def _displace(x, off_int):
            _, _, _, h, w = x.shape

            def shift_one(xp, dxy):
                dx, dy = (dxy[0], dxy[1])
                ys = jnp.arange(h) - dy
                xs = jnp.arange(w) - dx
                ym = (ys >= 0) & (ys < h)
                xm = (xs >= 0) & (xs < w)
                ysc = jnp.clip(ys, 0, h - 1)
                xsc = jnp.clip(xs, 0, w - 1)
                out = xp[:, :, ysc][:, :, :, xsc]
                return out * (ym[:, None] & xm[None, :]).astype(xp.dtype)
            return jax.vmap(shift_one, in_axes=(1, 0), out_axes=1)(x, off_int)
        B, C, h, w = x.shape
        P = offset.shape[0]
        cpp = C // P
        off_round = jnp.round(offset)
        off_int = off_round.astype(jnp.int32)
        disp = _displace(x.reshape(B, P, cpp, h, w), off_int).reshape(B, C, h, w)
        sub = offset - lax.stop_gradient(off_round)
        c = K // 2
        jj, ii = jnp.meshgrid(jnp.arange(K, dtype=jnp.float32) - c, jnp.arange(K, dtype=jnp.float32) - c, indexing='xy')
        field = jnp.stack([jj, ii], axis=-1)
        d = field[None] + sub[:, None, None, :]
        kernel = jnp.exp(-jnp.sum(d * d, axis=-1) / (2.0 * SIGMA ** 2))
        kernel = kernel / jnp.sum(kernel, axis=(1, 2), keepdims=True)
        kw = jnp.repeat(kernel, cpp, axis=0)[:, None]
        out = lax.conv_general_dilated(disp, kw, window_strides=(1, 1), padding=[(c, c), (c, c)], feature_group_count=C, dimension_numbers=('NCHW', 'OIHW', 'NCHW'))
        return out

    def _gn(v, G=32, eps=1e-5):
        B_, C_, H_, W_ = v.shape
        g = v.reshape(B_, G, C_ // G, H_, W_)
        m = jnp.mean(g, axis=(2, 3, 4), keepdims=True)
        s = jnp.var(g, axis=(2, 3, 4), keepdims=True)
        return ((g - m) / jnp.sqrt(s + eps)).reshape(v.shape)

    def _ln_c(v, eps=1e-6):
        m = jnp.mean(v, axis=1, keepdims=True)
        s = jnp.var(v, axis=1, keepdims=True)
        return (v - m) / jnp.sqrt(s + eps)

    def _ln_t(v, eps=1e-5):
        m = jnp.mean(v, axis=-1, keepdims=True)
        s = jnp.var(v, axis=-1, keepdims=True)
        return (v - m) / jnp.sqrt(s + eps)

    def _to_tokens(v):
        B_, C_, H_, W_ = v.shape
        return v.reshape(B_, C_, H_ * W_).transpose(0, 2, 1)
    def _from_tokens(t, like):
        B_, C_, H_, W_ = like.shape
        return t.transpose(0, 2, 1).reshape(B_, C_, H_, W_)

    x = x + _L0_conv_ref(_gn(x), L0_conv_offset)
    return x


_drawn_inputs = setup_inputs


def setup_inputs(seed=0):
    import zlib

    import numpy as np

    out = dict(_drawn_inputs(seed))
    spreads = {}
    factors = {}
    for name, (base, spread) in spreads.items():
        noise = np.random.default_rng([zlib.crc32(name.encode()), seed]).standard_normal(out[name].shape)
        drawn = base * np.exp(spread * noise) if base else spread * noise
        out[name] = jnp.asarray(drawn.astype(out[name].dtype))
    for name, factor in factors.items():
        out[name] = (out[name] * factor).astype(out[name].dtype)
    return out
```

```python
import concourse.bass as bass
from concourse import mybir
from contextlib import ExitStack

F32 = mybir.dt.float32
F16 = mybir.dt.float16
I32 = mybir.dt.int32
ALU = mybir.AluOpType
ACT = mybir.ActivationFunctionType
AX = mybir.AxisListType

BATCH, CH, HW = 32, 384, 64
P = 128
POSITIONS = 48
QUAD = 4
SUPER = 24
NSUPER = CH // SUPER
Q = SUPER // QUAD
POS = 3
GROUPS = 2
QG = Q // GROUPS
B = 2
STEPS = BATCH // B
BODY = 4
ROW = 2 * HW
COLS = Q * 2 * B * HW
HALF = COLS // GROUPS
EPS = 1e-5
TAPS = 5
ROUND = 12582912.0
FAR = 200.0


def displaced_conv(nc: bass.Bass, x: bass.AP, offset: bass.AP, out: bass.AP):
    def tiled(a):
        return (a.rearrange("n c h w -> n (c h w)")
                 .rearrange("(m i b) (s q p f) -> m i b s p q f", i=BODY, b=B, s=NSUPER, q=Q, p=P))

    x_t, out_t = tiled(x), tiled(out)
    off_row = offset.rearrange("(o p) k -> o (p k)", o=1)

    with ExitStack() as ctx:
        def sb(name, shape, dt=F32):
            return ctx.enter_context(nc.sbuf_tensor(name, shape, dt))

        def sem(name):
            return ctx.enter_context(nc.semaphore(name))

        xin = sb("xin", [P, BODY, B, Q, ROW])
        norm = sb("norm", [P, 2, Q * 2, B, HW])
        norm_hi = sb("norm_hi", [P, 2, Q * 2, B, HW], F16)
        norm_lo = sb("norm_lo", [P, 2, Q * 2, B, HW], F16)
        y_hi = sb("y_hi", [P, POS, 2, 2, P], F16)
        y_lo = sb("y_lo", [P, POS, 2, 2, P], F16)
        result = sb("result", [P, 2, B, Q, ROW])
        stats = sb("stats", [P, 2, B * GROUPS, 6])
        sums = sb("sums", [P, 2, B * GROUPS, 6])
        tot = sb("tot", [P, 2, B * GROUPS, 3])
        mean2 = sb("mean2", [P, 2, B * GROUPS])
        var_a = sb("var_a", [P, 2, B * GROUPS])
        var_b = sb("var_b", [P, 2, B * GROUPS])
        var_d = sb("var_d", [P, 2, B * GROUPS])
        var_c = sb("var_c", [P, 2, B * GROUPS])
        rstd = sb("rstd", [P, 2, B * GROUPS])
        nmean = sb("nmean", [P, 2, B * GROUPS])
        bias = sb("bias", [P, 2, B * GROUPS])
        ones = sb("ones", [P, P])
        mhalf = sb("mhalf", [P, B * GROUPS])
        minus_one = sb("minus_one", [P, B * GROUPS])
        per_half = sb("per_half", [P, B * GROUPS])
        epsilon = sb("epsilon", [P, B * GROUPS])
        ay_hi = sb("ay_hi", [P, 2, POS, 2, 2 * P], F16)
        ay_lo = sb("ay_lo", [P, 2, POS, 2, 2 * P], F16)
        ax_hi = sb("ax_hi", [P, 2, POS, P], F16)
        ax_lo = sb("ax_lo", [P, 2, POS, P], F16)
        grid_i = sb("grid_i", [P, 3, HW], I32)
        grid = sb("grid", [P, 3, HW])
        src_i = sb("src_i", [P, 3], I32)
        src = sb("src", [P, 3])
        off = sb("off", [P, POSITIONS, 2])
        offc = sb("offc", [P, POSITIONS, 2])
        rnd_a = sb("rnd_a", [P, POSITIONS, 2])
        rnd = sb("rnd", [P, POSITIONS, 2])
        sub = sb("sub", [P, POSITIONS, 2])
        tap = sb("tap", [P, TAPS, POSITIONS * 2])
        tap_sq = sb("tap_sq", [P, TAPS, POSITIONS * 2])
        tap_e = sb("tap_e", [P, TAPS, POSITIONS * 2])
        tap_sum = sb("tap_sum", [P, POSITIONS, 2])
        tap_inv = sb("tap_inv", [P, POSITIONS, 2])
        shift3 = sb("shift3", [P, POSITIONS, 3])
        sub3 = sb("sub3", [P, POSITIONS, 3])
        inv3 = sb("inv3", [P, POSITIONS, 3])
        place3 = sb("place3", [P, POSITIONS, 3])
        ok_lo = sb("ok_lo", [P, POSITIONS, 3])
        ok_hi = sb("ok_hi", [P, POSITIONS, 3])
        valid3 = sb("valid3", [P, POSITIONS, 3])
        gain3 = sb("gain3", [P, POSITIONS, 3])
        t_int = sb("t_int", [P, POS, 3, HW])
        t_full = sb("t_full", [P, POS, 3, HW])
        t_isq = sb("t_isq", [P, POS, 3, HW])
        t_fsq = sb("t_fsq", [P, POS, 3, HW])
        t_exp = sb("t_exp", [P, POS, 3, HW])
        t_msk = sb("t_msk", [P, POS, 3, HW])
        t_val = sb("t_val", [P, POS, 3, HW])
        t_hi = sb("t_hi", [P, POS, 3, HW], F16)
        t_lo = sb("t_lo", [P, POS, 3, HW], F16)

        yp = [ctx.enter_context(nc.psum_tensor(f"yp{k}", [P, 2, 2 * P], F32)) for k in range(POS)]
        xp = [ctx.enter_context(nc.psum_tensor(f"xp{k}", [P, B, 2, 2, HW], F32)) for k in range(POS)]
        sp_ = ctx.enter_context(nc.psum_tensor("sp_", [P, 512], F32))

        loaded = [sem(f"loaded{i}") for i in range(BODY)]
        stored = [sem(f"stored{i}") for i in range(2)]
        off_loaded = sem("off_loaded")
        bn_done = sem("bn_done")
        stats_ready = sem("stats_ready")
        stat_summed = sem("stat_summed")
        sums_ready = sem("sums_ready")
        small = sem("small")
        coef_ready = sem("coef_ready")
        norm_ready = sem("norm_ready")
        lo_ready = sem("lo_ready")
        y_done = sem("y_done")
        y_hi_ready = sem("y_hi_ready")
        y_lo_ready = sem("y_lo_ready")
        x_done = sem("x_done")
        result_ready = sem("result_ready")
        consts = sem("consts")
        prep = sem("prep")
        taps_sq = sem("taps_sq")
        taps_exp = sem("taps_exp")
        gains = sem("gains")
        dist_ready = sem("dist_ready")
        sq_ready = sem("sq_ready")
        exp_ready = sem("exp_ready")
        made = sem("made")
        mats_ready = sem("mats_ready")

        block = ctx.enter_context(nc.Block())

        def run(eng, step, extra=None):
            def superblock(c, buf, head=False, tail=False):
                def body(t0, lead=False, end=False):
                    for i in range(BODY):
                        step(t0, i, c, buf, head and lead, lead, end, tail)
                body(16 * c, lead=True)
                if tail:
                    with eng.Fori(16 * c + BODY, 16 * c + STEPS - BODY, BODY) as t0:
                        body(t0)
                    body(16 * c + STEPS - BODY, end=True)
                else:
                    with eng.Fori(16 * c + BODY, 16 * c + STEPS, BODY) as t0:
                        body(t0)
            superblock(0, 0, head=True)
            with eng.Fori(0, NSUPER // 2 - 1) as m:
                superblock(2 * m + 1, 1)
                superblock(2 * m + 2, 0)
            superblock(NSUPER - 1, 1, tail=True)

        @block.sync
        def _(sync):
            sync.dma_start(off[:, :, :], off_row.to_broadcast([P, 2 * POSITIONS])).then_inc(off_loaded, 16)

            def load(m, i, c):
                for b in range(B):
                    sync.dma_start(xin[:, i, b], x_t[m, i, b, c]).then_inc(loaded[i], 16)

            def store(m, i, c):
                for b in range(B):
                    sync.dma_start(out_t[m, i, b, c], result[:, i % 2, b]).then_inc(stored[i % 2], 16)

            def body(c, m, c_next, m_next):
                for i in range(BODY):
                    sync.wait_ge(result_ready, POS * (STEPS * c + BODY * m + i + 1))
                    store(m, i, c)
                    if m_next is not None:
                        load(m_next, i, c_next)

            BODIES = STEPS // BODY
            for i in range(BODY):
                load(0, i, 0)
            with sync.Fori(0, NSUPER - 1) as c:
                with sync.Fori(0, BODIES - 1) as m:
                    body(c, m, c, m + 1)
                body(c, BODIES - 1, c + 1, 0)
            with sync.Fori(0, BODIES - 1) as m:
                body(NSUPER - 1, m, NSUPER - 1, m + 1)
            body(NSUPER - 1, BODIES - 1, None, None)
            for i in range(2):
                sync.wait_ge(stored[i], 16 * B * NSUPER * STEPS // 2)

        SMALLS = 8
        CONSTS = 2 * QUAD + 2 * B + 9

        @block.gpsimd
        def _(pool):
            for a in range(QUAD):
                rows = slice(32 * a, 32 * a + 32)
                pool.iota(grid_i[rows, 0:2, :], pattern=[[1, 2], [-1, 2], [-2, 32]], base=0,
                          channel_multiplier=2).then_inc(consts, 1)
                pool.iota(src_i[rows, 0:2], pattern=[[1, 2]], base=0, channel_multiplier=2).then_inc(consts, 1)
            pool.wait_ge(consts, 2 * QUAD)
            for b in range(B):
                rows = slice(64 * b, 64 * b + 64)
                pool.iota(grid_i[rows, 2:3, :], pattern=[[0, 1], [-1, HW]], base=0,
                          channel_multiplier=1).then_inc(consts, 1)
                pool.iota(src_i[rows, 2:3], pattern=[[0, 1]], base=0, channel_multiplier=1).then_inc(consts, 1)
            pool.wait_ge(consts, 2 * QUAD + 2 * B)
            pool.memset(ones[:, :], 1.0 / (2 * P)).then_inc(consts, 1)
            for tile, value in ((mhalf, -0.5), (minus_one, -1.0), (per_half, 2.0 / (QG * ROW)), (epsilon, EPS)):
                pool.memset(tile[:, :], value).then_inc(consts, 1)
            for m in (ay_hi, ay_lo, ax_hi, ax_lo):
                pool.memset(m[:], 0.0).then_inc(consts, 1)

            def distances(c):
                if c is 0:
                    pool.wait_ge(gains, 1)
                else:
                    pool.wait_ge(mats_ready, c)
                at = bass.ds(POS * c, POS)
                pool.tensor_tensor(t_int[:], grid[:, None, :, :].to_broadcast([P, POS, 3, HW]),
                                   shift3[:, at, :].unsqueeze(3).to_broadcast([P, POS, 3, HW]),
                                   ALU.add).then_inc(dist_ready, 1)
                pool.wait_ge(dist_ready, 2 * c + 1)
                pool.tensor_tensor(t_full[:], t_int[:],
                                   sub3[:, at, :].unsqueeze(3).to_broadcast([P, POS, 3, HW]),
                                   ALU.add).then_inc(dist_ready, 1)

            def coefficients(t, v):
                n = [SMALLS * t]

                def own(ins):
                    n[0] = n[0] + 1
                    ins.then_inc(small, 1)
                    pool.wait_ge(small, n[0])

                pool.wait_ge(sums_ready, t + 1)
                own(pool.tensor_tensor(tot[:, v], sums[:, v, :, 0:3], sums[:, v, :, 3:6], ALU.add))
                own(pool.tensor_tensor(mean2[:, v], tot[:, v, :, 1], tot[:, v, :, 1], ALU.mult))
                own(pool.tensor_tensor(nmean[:, v], tot[:, v, :, 1], minus_one[:, :], ALU.mult))
                own(pool.tensor_tensor(var_a[:, v], tot[:, v, :, 2], per_half[:, :], ALU.mult))
                own(pool.tensor_tensor(var_b[:, v], var_a[:, v], tot[:, v, :, 0], ALU.add))
                own(pool.tensor_tensor(var_c[:, v], var_b[:, v], mean2[:, v], ALU.subtract))
                own(pool.tensor_tensor(var_d[:, v], var_c[:, v], epsilon[:, :], ALU.add))
                own(pool.tensor_tensor(rstd[:, v], var_d[:, v], mhalf[:, :], ALU.pow))
                pool.tensor_tensor(bias[:, v], nmean[:, v], rstd[:, v], ALU.mult).then_inc(coef_ready, 1)

            def low_part(t, v):
                for g in range(GROUPS):
                    pool.wait_ge(norm_ready, 2 * B * GROUPS * t + 2 * B * (g + 1))
                    cols = slice(2 * QG * g, 2 * QG * (g + 1))
                    pool.tensor_tensor(norm_lo[:, v, cols], norm[:, v, cols], norm_hi[:, v, cols],
                                       ALU.subtract).then_inc(lo_ready, 1)

            distances(0)
            coefficients(0, 0)
            low_part(0, 0)

            def step(t0, i, c, buf, head, lead, end, tail):
                if lead and i == 1 and not tail:
                    distances(c + 1)
                if end and i == BODY - 1:
                    return
                coefficients(t0 + i + 1, (i + 1) % 2)
                low_part(t0 + i + 1, (i + 1) % 2)
            run(pool, step)

        @block.vector
        def _(dve):
            n = [0]

            def own(ins):
                n[0] += 1
                ins.then_inc(prep, 1)
                dve.wait_ge(prep, n[0])

            def tsc(o, i, s1, s2, op0, op1):
                own(nc.vector.tensor_scalar(o, i, s1, s2, op0, op1))

            dve.wait_ge(consts, CONSTS)
            own(nc.vector.tensor_copy(grid[:], grid_i[:]))
            own(nc.vector.tensor_copy(src[:], src_i[:]))
            dve.wait_ge(off_loaded, 16)
            tsc(offc[:], off[:], FAR, -FAR, ALU.min, ALU.max)
            tsc(rnd_a[:], offc[:], ROUND, 0.0, ALU.add, ALU.add)
            tsc(rnd[:], rnd_a[:], -ROUND, 0.0, ALU.add, ALU.add)
            own(nc.vector.tensor_tensor(sub[:], offc[:], rnd[:], ALU.subtract))
            for k in range(TAPS):
                tsc(tap[:, k, :], sub[:].rearrange("p n k -> p (n k)"), float(k - TAPS // 2), 0.0, ALU.add, ALU.add)
            nc.vector.engine_nop().then_inc(taps_sq, 1)
            for kind in range(3):
                axis = 1 if kind < 2 else 0
                own(nc.vector.tensor_copy(shift3[:, :, kind], rnd[:, :, axis]))
                own(nc.vector.tensor_copy(sub3[:, :, kind], sub[:, :, axis]))
            own(nc.vector.tensor_tensor(place3[:], shift3[:],
                                        src[:, None, :].to_broadcast([P, POSITIONS, 3]), ALU.add))
            tsc(ok_lo[:], place3[:], 0.0, 0.0, ALU.is_ge, ALU.add)
            tsc(ok_hi[:], place3[:], float(HW - 1), 0.0, ALU.is_le, ALU.add)
            own(nc.vector.tensor_tensor(valid3[:], ok_lo[:], ok_hi[:], ALU.mult))
            dve.wait_ge(taps_exp, 1)
            own(nc.vector.tensor_reduce(tap_sum[:].rearrange("p n k -> p (n k)"),
                                        tap_e[:].rearrange("p t m -> p m t"), AX.X, ALU.add))
            own(nc.vector.reciprocal(tap_inv[:], tap_sum[:]))
            for kind in range(3):
                own(nc.vector.tensor_copy(inv3[:, :, kind], tap_inv[:, :, 1 if kind < 2 else 0]))
            nc.vector.tensor_tensor(gain3[:], valid3[:], inv3[:], ALU.mult).then_inc(gains, 1)

            MADES = 4

            def matrices(c, buf, wait_x):
                dve.wait_ge(exp_ready, c + 1)
                nc.vector.scalar_tensor_tensor(out=t_msk[:].rearrange("p a k w -> p (a k w)"),
                                               in0=t_isq[:].rearrange("p a k w -> p (a k w)"), scalar=4.0,
                                               in1=t_exp[:].rearrange("p a k w -> p (a k w)"),
                                               op0=ALU.is_le, op1=ALU.mult).then_inc(made, 1)
                dve.wait_ge(made, MADES * c + 1)
                if c is 0:
                    dve.wait_ge(gains, 1)
                nc.vector.tensor_tensor(t_val[:], t_msk[:],
                                        gain3[:, bass.ds(POS * c, POS), :].unsqueeze(3).to_broadcast([P, POS, 3, HW]),
                                        ALU.mult).then_inc(made, 1)
                dve.wait_ge(made, MADES * c + 2)
                nc.vector.tensor_copy(t_hi[:], t_val[:]).then_inc(made, 1)
                dve.wait_ge(made, MADES * c + 3)
                nc.vector.tensor_tensor(t_lo[:], t_val[:], t_hi[:], ALU.subtract).then_inc(made, 1)
                dve.wait_ge(made, MADES * c + 4)
                if wait_x is not None:
                    dve.wait_ge(x_done, wait_x)
                for t_part, ay, ax in ((t_hi, ay_hi, ax_hi), (t_lo, ay_lo, ax_lo)):
                    for a in range(QUAD):
                        rows = slice(32 * a, 32 * a + 32)
                        nc.vector.tensor_copy(
                            ay[rows, buf].rearrange("p n r (s a j) -> p n (r s) a j", s=2, a=QUAD)[:, :, :, a, :],
                            t_part[rows, :, 0:2, :].rearrange("p n r (s j) -> p n (r s) j", s=2))
                    for b in range(B):
                        rows = slice(64 * b, 64 * b + 64)
                        last = nc.vector.tensor_copy(ax[rows, buf, :, 64 * b:64 * b + 64], t_part[rows, :, 2, :])
                last.then_inc(mats_ready, 1)

            def statistics(t, i, part, first=False):
                if part == 0:
                    dve.wait_ge(loaded[i], 8 * (t - i) + 32)
                    if not first:
                        dve.wait_ge(stat_summed, t - 1)
                v = i % 2
                for g in range(GROUPS):
                    nc.vector.bn_stats(stats[:, v, GROUPS * part + g, :],
                                       xin[:, i, part, QG * g:QG * (g + 1), :].rearrange("p q f -> p (q f)")
                                       ).then_inc(bn_done, 1)
                if part == B - 1:
                    dve.wait_ge(bn_done, B * GROUPS * (t + 1))
                    nc.vector.tensor_tensor(stats[:, v, :, 0:6:3], stats[:, v, :, 1:6:3], stats[:, v, :, 1:6:3],
                                            ALU.mult).then_inc(stats_ready, 1)

            def low_part(t, k):
                dve.wait_ge(y_hi_ready, POS * t + k + 1)
                nc.vector.tensor_tensor(y_lo[:, k].rearrange("p q r m -> p (q r m)"),
                                        yp[k][:].rearrange("p q m -> p (q m)"),
                                        y_hi[:, k].rearrange("p q r m -> p (q r m)"),
                                        ALU.subtract).then_inc(y_lo_ready, 1)

            def add_x(t, i, k):
                dve.wait_ge(x_done, POS * t + k + 1)
                nc.vector.tensor_tensor(result[:, i % 2, :, 2 * k:2 * k + 2, :].rearrange("p b q f -> p b (q f)"),
                                        xp[k][:].rearrange("p b q r w -> p b (q r w)"),
                                        xin[:, i, :, 2 * k:2 * k + 2, :].rearrange("p b q f -> p b (q f)"),
                                        ALU.add).then_inc(result_ready, 1)

            matrices(0, 0, None)
            statistics(0, 0, 0, first=True)
            statistics(0, 0, 1)

            def step(t0, i, c, buf, head, lead, end, tail):
                t = t0 + i
                more = not (end and i == BODY - 1)
                low_part(t, 0)
                if more:
                    statistics(t + 1, (i + 1) % BODY, 0, first=head and i == 0)
                if not (head and i == 0):
                    add_x(t - 1, (i - 1) % BODY, 2)
                if more:
                    statistics(t + 1, (i + 1) % BODY, 1)
                low_part(t, 1)
                if not (head and i < 2):
                    dve.wait_ge(stored[i % 2], 16 * (t - i % 2))
                add_x(t, i, 0)
                low_part(t, 2)
                add_x(t, i, 1)
                if lead and i == 1 and not tail:
                    matrices(c + 1, 1 - buf, None if head else POS * STEPS * c)
            run(dve, step)
            add_x(NSUPER * STEPS - 1, BODY - 1, 2)

        @block.scalar
        def _(act):
            act.wait_ge(taps_sq, 1)
            nc.scalar.activation(tap_sq[:], tap[:], ACT.Square).then_inc(taps_sq, 1)
            act.wait_ge(taps_sq, 2)
            nc.scalar.activation(tap_e[:], tap_sq[:], ACT.Exp, scale=-2.0).then_inc(taps_exp, 1)

            def squares(c):
                act.wait_ge(dist_ready, 2 * c + 2)
                nc.scalar.activation(t_isq[:], t_int[:], ACT.Square).then_inc(sq_ready, 1)
                nc.scalar.activation(t_fsq[:], t_full[:], ACT.Square).then_inc(sq_ready, 1)
                act.wait_ge(sq_ready, 2 * c + 2)
                nc.scalar.activation(t_exp[:], t_fsq[:], ACT.Exp, scale=-2.0).then_inc(exp_ready, 1)

            def copy_sums(t, v):
                act.wait_ge(stat_summed, t + 1)
                nc.scalar.activation(sums[:, v].rearrange("p g s -> p (g s)"), sp_[:, 0:6 * B * GROUPS],
                                     ACT.Copy).then_inc(sums_ready, 1)

            def normalise(t, i, g, first):
                if g == 0:
                    act.wait_ge(coef_ready, t + 1)
                    if not first:
                        act.wait_ge(y_done, POS * (t - 1))
                v = i % 2
                for b in range(B):
                    col = GROUPS * b + g
                    for o in (norm, norm_hi):
                        nc.scalar.activation(o[:, v, 2 * QG * g:2 * QG * (g + 1), b, :],
                                             xin[:, i, b, QG * g:QG * (g + 1), :].rearrange("p q (r w) -> p (q r) w", r=2),
                                             ACT.Identity, bias=bias[:, v, col:col + 1],
                                             scale=rstd[:, v, col:col + 1]).then_inc(norm_ready, 1)

            def high_part(t, k, first):
                act.wait_ge(y_done, POS * t + k + 1)
                if not first:
                    act.wait_ge(x_done, POS * (t - 1) + k + 1)
                nc.scalar.activation(y_hi[:, k].rearrange("p q r m -> p (q r m)"),
                                     yp[k][:].rearrange("p q m -> p (q m)"), ACT.Copy).then_inc(y_hi_ready, 1)

            squares(0)
            copy_sums(0, 0)
            normalise(0, 0, 0, True)
            normalise(0, 0, 1, True)

            def step(t0, i, c, buf, head, lead, end, tail):
                t = t0 + i
                first = head and i == 0
                more = not (end and i == BODY - 1)
                high_part(t, 0, first)
                high_part(t, 1, first)
                if more:
                    copy_sums(t + 1, (i + 1) % 2)
                    normalise(t + 1, (i + 1) % BODY, 0, first)
                high_part(t, 2, first)
                if more:
                    normalise(t + 1, (i + 1) % BODY, 1, first)
                if lead and i == 1 and not tail:
                    squares(c + 1)
            run(act, step)

        @block.tensor
        def _(pe):
            def products(dst, pairs):
                for m, (w, mov) in enumerate(pairs):
                    last = nc.tensor.matmul(dst, w, mov, start=(m == 0), stop=(m == len(pairs) - 1))
                return last

            def sum_stats(t, v, first=False):
                pe.wait_ge(stats_ready, t + 1)
                if not first:
                    pe.wait_ge(sums_ready, t)
                nc.tensor.matmul(sp_[:, 0:6 * B * GROUPS], ones[:, :], stats[:, v].rearrange("p g s -> p (g s)"),
                                 start=True, stop=True).then_inc(stat_summed, 1)

            def y_product(t, i, k, buf, first):
                if k < 2:
                    pe.wait_ge(lo_ready, GROUPS * t + k + 1)
                if not first:
                    pe.wait_ge(y_lo_ready, POS * (t - 1) + k + 1)
                v = i % 2
                for q in range(2):
                    pairs = []
                    for r in range(2):
                        hi, lo = (o[:, v, 2 * (2 * k + q) + r].rearrange("p b w -> p (b w)") for o in (norm_hi, norm_lo))
                        pairs += [(hi, ay_hi[:, buf, k, r]), (hi, ay_lo[:, buf, k, r]), (lo, ay_hi[:, buf, k, r])]
                    last = products(yp[k][:, q], pairs)
                last.then_inc(y_done, 1)

            def x_product(t, k, buf, first):
                pe.wait_ge(y_lo_ready, POS * t + k + 1)
                if not first:
                    pe.wait_ge(result_ready, POS * (t - 1) + k + 1)
                for q in range(2):
                    for r in range(2):
                        hi, lo = y_hi[:, k, q, r], y_lo[:, k, q, r]
                        last = products(xp[k][:, :, q, r, :], [(hi, ax_hi[:, buf, k]), (hi, ax_lo[:, buf, k]),
                                                               (lo, ax_hi[:, buf, k])])
                last.then_inc(x_done, 1)

            pe.wait_ge(consts, CONSTS)
            sum_stats(0, 0, first=True)

            def step(t0, i, c, buf, head, lead, end, tail):
                t = t0 + i
                first = head and i == 0
                if lead and i == 0:
                    pe.wait_ge(mats_ready, c + 1)
                y_product(t, i, 0, buf, first)
                if not first:
                    x_product(t - 1, 2, 1 - buf if lead and i == 0 else buf, head and i == 1)
                y_product(t, i, 1, buf, first)
                if not (end and i == BODY - 1):
                    sum_stats(t + 1, (i + 1) % 2)
                x_product(t, 0, buf, first)
                y_product(t, i, 2, buf, first)
                x_product(t, 1, buf, first)
            run(pe, step)
            x_product(NSUPER * STEPS - 1, 2, 1, False)


_INS = ["x", "L0_conv_offset"]


def kernel(**inputs):
    import numpy as _np
    import concourse.bacc as _bacc
    from concourse import mybir as _mybir
    from concourse.bass_utils import run_bass_kernel_spmd as _run

    nc = _bacc.Bacc("TRN2", target_bir_lowering=False, num_devices=1)
    arrays, args = {}, []
    for name in _INS:
        a = _np.ascontiguousarray(inputs[name])
        arrays[f"in_{name}_dram"] = a
        args.append(nc.dram_tensor(f"in_{name}_dram", a.shape, _mybir.dt.from_np(a.dtype), kind="ExternalInput").ap())
    args.append(nc.dram_tensor("out_dram", (BATCH, CH, HW, HW), F32, kind="ExternalOutput").ap())
    displaced_conv(nc, *args)
    r = _run(nc, [arrays], core_ids=[0])
    return r.results[0]["out_dram"]
```

```python
import concourse.bass as bass
from concourse import mybir
from contextlib import ExitStack

F32 = mybir.dt.float32
F16 = mybir.dt.float16
I32 = mybir.dt.int32
ALU = mybir.AluOpType
ACT = mybir.ActivationFunctionType
AX = mybir.AxisListType

BATCH, CH, HW = 32, 384, 64
P = 128
POSITIONS = 48
QUAD = 4
SUPER = 24
NSUPER = CH // SUPER
Q = SUPER // QUAD
POS = 3
GROUPS = 2
QG = Q // GROUPS
B = 2
STEPS = BATCH // B
BODY = 8
SLOTS = 4
LAG = 2
ROW = 2 * HW
COLS = Q * 2 * B * HW
HALF = COLS // GROUPS
EPS = 1e-5
TAPS = 5
ROUND = 12582912.0
FAR = 200.0


def displaced_conv(nc: bass.Bass, x: bass.AP, offset: bass.AP, out: bass.AP):
    def tiled(a):
        return (a.rearrange("n c h w -> n (c h w)")
                 .rearrange("(m i b) (s q p f) -> m i b s p q f", i=BODY, b=B, s=NSUPER, q=Q, p=P))

    x_t, out_t = tiled(x), tiled(out)
    off_row = offset.rearrange("(o p) k -> o (p k)", o=1)

    with ExitStack() as ctx:
        def sb(name, shape, dt=F32):
            return ctx.enter_context(nc.sbuf_tensor(name, shape, dt))

        def sem(name):
            return ctx.enter_context(nc.semaphore(name))

        xin = sb("xin", [P, BODY, B, Q, ROW])
        norm = sb("norm", [P, 2, Q * 2, B, HW])
        norm_hi = sb("norm_hi", [P, 2, Q * 2, B, HW], F16)
        norm_lo = sb("norm_lo", [P, 2, Q * 2, B, HW], F16)
        y_hi = sb("y_hi", [P, POS, 2, 2, P], F16)
        y_lo = sb("y_lo", [P, POS, 2, 2, P], F16)
        result = sb("result", [P, SLOTS, B, Q, ROW])
        stats = sb("stats", [P, 4, B * GROUPS, 6])
        parts = sb("parts", [P, 2, 4, 2 * B * GROUPS])
        spread = sb("spread", [P, 2, 2 * B * GROUPS])
        var = sb("var", [P, 2, 2 * B * GROUPS])
        rstd = sb("rstd", [P, 2, 2 * B * GROUPS])
        bias = sb("bias", [P, 2, 2 * B * GROUPS])
        ones = sb("ones", [P, P])
        mhalf = sb("mhalf", [P, 2 * B * GROUPS])
        ay_hi = sb("ay_hi", [P, 2, POS, 2, 2 * P], F16)
        ay_lo = sb("ay_lo", [P, 2, POS, 2, 2 * P], F16)
        ax_hi = sb("ax_hi", [P, 2, POS, P], F16)
        ax_lo = sb("ax_lo", [P, 2, POS, P], F16)
        grid_i = sb("grid_i", [P, 3, HW], I32)
        grid = sb("grid", [P, 3, HW])
        src_i = sb("src_i", [P, 3], I32)
        src = sb("src", [P, 3])
        off = sb("off", [P, POSITIONS, 2])
        offc = sb("offc", [P, POSITIONS, 2])
        rnd_a = sb("rnd_a", [P, POSITIONS, 2])
        rnd = sb("rnd", [P, POSITIONS, 2])
        sub = sb("sub", [P, POSITIONS, 2])
        tap = sb("tap", [P, TAPS, POSITIONS * 2])
        tap_sq = sb("tap_sq", [P, TAPS, POSITIONS * 2])
        tap_e = sb("tap_e", [P, TAPS, POSITIONS * 2])
        tap_sum = sb("tap_sum", [P, POSITIONS, 2])
        tap_inv = sb("tap_inv", [P, POSITIONS, 2])
        shift3 = sb("shift3", [P, POSITIONS, 3])
        sub3 = sb("sub3", [P, POSITIONS, 3])
        inv3 = sb("inv3", [P, POSITIONS, 3])
        place3 = sb("place3", [P, POSITIONS, 3])
        ok_lo = sb("ok_lo", [P, POSITIONS, 3])
        ok_hi = sb("ok_hi", [P, POSITIONS, 3])
        valid3 = sb("valid3", [P, POSITIONS, 3])
        gain3 = sb("gain3", [P, POSITIONS, 3])
        t_int = sb("t_int", [P, POS, 3, HW])
        t_full = sb("t_full", [P, POS, 3, HW])
        t_isq = sb("t_isq", [P, POS, 3, HW])
        t_fsq = sb("t_fsq", [P, POS, 3, HW])
        t_exp = sb("t_exp", [P, POS, 3, HW])
        t_msk = sb("t_msk", [P, POS, 3, HW])
        t_val = sb("t_val", [P, POS, 3, HW])
        t_hi = sb("t_hi", [P, POS, 3, HW], F16)
        t_lo = sb("t_lo", [P, POS, 3, HW], F16)

        yp = [ctx.enter_context(nc.psum_tensor(f"yp{k}", [P, 2, 2 * P], F32)) for k in range(POS)]
        xp = [ctx.enter_context(nc.psum_tensor(f"xp{k}", [P, B, 2, 2, HW], F32)) for k in range(POS)]
        sp_ = ctx.enter_context(nc.psum_tensor("sp_", [P, 512], F32))

        loaded = [sem(f"loaded{i}") for i in range(BODY)]
        stored = [sem(f"stored{i}") for i in range(SLOTS)]
        off_loaded = sem("off_loaded")
        bn_done = sem("bn_done")
        stats_ready = sem("stats_ready")
        stat_summed = sem("stat_summed")
        parts_ready = sem("parts_ready")
        small = sem("small")
        coef_ready = sem("coef_ready")
        norm_ready = sem("norm_ready")
        hi_ready = sem("hi_ready")
        lo_ready = sem("lo_ready")
        y_done = sem("y_done")
        y_hi_ready = sem("y_hi_ready")
        y_lo_ready = sem("y_lo_ready")
        x_done = sem("x_done")
        result_ready = sem("result_ready")
        consts = sem("consts")
        prep = sem("prep")
        taps_sq = sem("taps_sq")
        taps_exp = sem("taps_exp")
        gains = sem("gains")
        dist_ready = sem("dist_ready")
        sq_ready = sem("sq_ready")
        exp_ready = sem("exp_ready")
        made = sem("made")
        mats_ready = sem("mats_ready")

        block = ctx.enter_context(nc.Block())

        def run(eng, step):
            def superblock(c, buf, head=False, tail=False):
                for m in range(STEPS // BODY):
                    for i in range(BODY):
                        step(STEPS * c + BODY * m, STEPS // 2 * c + (BODY * m + i) // 2, i, c, buf,
                             head and m == 0, m == 0, tail and m == STEPS // BODY - 1)
            superblock(0, 0, head=True)
            with eng.Fori(0, NSUPER // 2 - 1) as n:
                superblock(2 * n + 1, 1)
                superblock(2 * n + 2, 0)
            superblock(NSUPER - 1, 1, tail=True)

        @block.sync
        def _(sync):
            sync.dma_start(off[:, :, :], off_row.to_broadcast([P, 2 * POSITIONS])).then_inc(off_loaded, 16)

            def load(m, i, c):
                for b in range(B):
                    sync.dma_start(xin[:, i, b], x_t[m, i, b, c]).then_inc(loaded[i], 16)

            def store(m, i, c):
                for b in range(B):
                    sync.dma_start(out_t[m, i, b, c], result[:, i % SLOTS, b]).then_inc(stored[i % SLOTS], 16)

            def body(c, m, c_next, m_next):
                for i in range(BODY):
                    sync.wait_ge(result_ready, POS * (STEPS * c + BODY * m + i + 1))
                    store(m, i, c)
                    if m_next is not None:
                        load(m_next, i, c_next)

            for i in range(BODY):
                load(0, i, 0)
            with sync.Fori(0, NSUPER - 1) as c:
                body(c, 0, c, 1)
                body(c, 1, c + 1, 0)
            body(NSUPER - 1, 0, NSUPER - 1, 1)
            body(NSUPER - 1, 1, None, None)
            for i in range(SLOTS):
                sync.wait_ge(stored[i], 16 * B * NSUPER * STEPS // SLOTS)

        SMALLS = 3
        MATS = 2 * (QUAD + B)
        CONSTS = 2 * QUAD + 2 * B + 6

        @block.gpsimd
        def _(pool):
            for a in range(QUAD):
                rows = slice(32 * a, 32 * a + 32)
                pool.iota(grid_i[rows, 0:2, :], pattern=[[1, 2], [-1, 2], [-2, 32]], base=0,
                          channel_multiplier=2).then_inc(consts, 1)
                pool.iota(src_i[rows, 0:2], pattern=[[1, 2]], base=0, channel_multiplier=2).then_inc(consts, 1)
            pool.wait_ge(consts, 2 * QUAD)
            for b in range(B):
                rows = slice(64 * b, 64 * b + 64)
                pool.iota(grid_i[rows, 2:3, :], pattern=[[0, 1], [-1, HW]], base=0,
                          channel_multiplier=1).then_inc(consts, 1)
                pool.iota(src_i[rows, 2:3], pattern=[[0, 1]], base=0, channel_multiplier=1).then_inc(consts, 1)
            pool.wait_ge(consts, 2 * QUAD + 2 * B)
            pool.memset(ones[:, :], 1.0 / (2 * P)).then_inc(consts, 1)
            pool.memset(mhalf[:, :], -0.5).then_inc(consts, 1)
            for m in (ay_hi, ay_lo, ax_hi, ax_lo):
                pool.memset(m[:], 0.0).then_inc(consts, 1)

            def distances(c):
                if c is 0:
                    pool.wait_ge(gains, 1)
                else:
                    pool.wait_ge(mats_ready, MATS * c)
                at = bass.ds(POS * c, POS)
                pool.tensor_tensor(t_int[:], grid[:, None, :, :].to_broadcast([P, POS, 3, HW]),
                                   shift3[:, at, :].unsqueeze(3).to_broadcast([P, POS, 3, HW]),
                                   ALU.add).then_inc(dist_ready, 1)
                pool.wait_ge(dist_ready, 2 * c + 1)
                pool.tensor_tensor(t_full[:], t_int[:],
                                   sub3[:, at, :].unsqueeze(3).to_broadcast([P, POS, 3, HW]),
                                   ALU.add).then_inc(dist_ready, 1)

            def coefficients(pair, v):
                n = [SMALLS * pair]

                def own(ins):
                    n[0] = n[0] + 1
                    ins.then_inc(small, 1)
                    pool.wait_ge(small, n[0])

                pool.wait_ge(parts_ready, 4 * (pair + 1))
                own(pool.tensor_tensor(spread[:, v], parts[:, v, 0], parts[:, v, 1], ALU.add))
                own(pool.tensor_tensor(var[:, v], spread[:, v], parts[:, v, 2], ALU.subtract))
                own(pool.tensor_tensor(rstd[:, v], var[:, v], mhalf[:, :], ALU.pow))
                pool.tensor_tensor(bias[:, v], parts[:, v, 3], rstd[:, v], ALU.mult).then_inc(coef_ready, 1)

            def low_part(t, v, g):
                pool.wait_ge(hi_ready, GROUPS * t + g + 1)
                cols = slice(2 * QG * g, 2 * QG * (g + 1))
                pool.tensor_tensor(norm_lo[:, v, cols], norm[:, v, cols], norm_hi[:, v, cols],
                                   ALU.subtract).then_inc(lo_ready, 1)

            distances(0)
            coefficients(0, 0)
            for g in range(GROUPS):
                low_part(0, 0, g)

            def step(t0, pair, i, c, buf, head, lead, end):
                more = not (end and i == BODY - 1)
                if more:
                    low_part(t0 + i + 1, (i + 1) % 2, 0)
                if i % 2 == 0 and not (end and i == BODY - 2):
                    coefficients(pair + 1, (i // 2 + 1) % 2)
                if more:
                    low_part(t0 + i + 1, (i + 1) % 2, 1)
                if lead and i == 1 and not isinstance(c, int) or lead and i == 1 and c < NSUPER - 1:
                    distances(c + 1)
            run(pool, step)

        @block.vector
        def _(dve):
            n = [0]

            def own(ins):
                n[0] += 1
                ins.then_inc(prep, 1)
                dve.wait_ge(prep, n[0])

            def tsc(o, i, s1, s2, op0, op1):
                own(nc.vector.tensor_scalar(o, i, s1, s2, op0, op1))

            dve.wait_ge(consts, CONSTS)
            own(nc.vector.tensor_copy(grid[:], grid_i[:]))
            own(nc.vector.tensor_copy(src[:], src_i[:]))
            dve.wait_ge(off_loaded, 16)
            tsc(offc[:], off[:], FAR, -FAR, ALU.min, ALU.max)
            tsc(rnd_a[:], offc[:], ROUND, 0.0, ALU.add, ALU.add)
            tsc(rnd[:], rnd_a[:], -ROUND, 0.0, ALU.add, ALU.add)
            own(nc.vector.tensor_tensor(sub[:], offc[:], rnd[:], ALU.subtract))
            for k in range(TAPS):
                tsc(tap[:, k, :], sub[:].rearrange("p n k -> p (n k)"), float(k - TAPS // 2), 0.0, ALU.add, ALU.add)
            nc.vector.engine_nop().then_inc(taps_sq, 1)
            for kind in range(3):
                axis = 1 if kind < 2 else 0
                own(nc.vector.tensor_copy(shift3[:, :, kind], rnd[:, :, axis]))
                own(nc.vector.tensor_copy(sub3[:, :, kind], sub[:, :, axis]))
            own(nc.vector.tensor_tensor(place3[:], shift3[:],
                                        src[:, None, :].to_broadcast([P, POSITIONS, 3]), ALU.add))
            tsc(ok_lo[:], place3[:], 0.0, 0.0, ALU.is_ge, ALU.add)
            tsc(ok_hi[:], place3[:], float(HW - 1), 0.0, ALU.is_le, ALU.add)
            own(nc.vector.tensor_tensor(valid3[:], ok_lo[:], ok_hi[:], ALU.mult))
            dve.wait_ge(taps_exp, 1)
            own(nc.vector.tensor_reduce(tap_sum[:].rearrange("p n k -> p (n k)"),
                                        tap_e[:].rearrange("p t m -> p m t"), AX.X, ALU.add))
            own(nc.vector.reciprocal(tap_inv[:], tap_sum[:]))
            for kind in range(3):
                own(nc.vector.tensor_copy(inv3[:, :, kind], tap_inv[:, :, 1 if kind < 2 else 0]))
            nc.vector.tensor_tensor(gain3[:], valid3[:], inv3[:], ALU.mult).then_inc(gains, 1)

            MADES = 4

            def matrices(c, buf, part, wait_x):
                if part == 0:
                    dve.wait_ge(exp_ready, c + 1)
                    nc.vector.scalar_tensor_tensor(out=t_msk[:].rearrange("p a k w -> p (a k w)"),
                                                   in0=t_isq[:].rearrange("p a k w -> p (a k w)"), scalar=4.0,
                                                   in1=t_exp[:].rearrange("p a k w -> p (a k w)"),
                                                   op0=ALU.is_le, op1=ALU.mult).then_inc(made, 1)
                    dve.wait_ge(made, MADES * c + 1)
                    nc.vector.tensor_tensor(t_val[:], t_msk[:],
                                            gain3[:, bass.ds(POS * c, POS), :].unsqueeze(3).to_broadcast([P, POS, 3, HW]),
                                            ALU.mult).then_inc(made, 1)
                if part == 1:
                    dve.wait_ge(made, MADES * c + 2)
                    nc.vector.tensor_copy(t_hi[:], t_val[:]).then_inc(made, 1)
                    dve.wait_ge(made, MADES * c + 3)
                    nc.vector.tensor_tensor(t_lo[:], t_val[:], t_hi[:], ALU.subtract).then_inc(made, 1)
                if part >= 2:
                    t_part, ay, ax = ((t_hi, ay_hi, ax_hi), (t_lo, ay_lo, ax_lo))[part - 2]
                    dve.wait_ge(made, MADES * c + 4)
                    if wait_x is not None:
                        dve.wait_ge(x_done, wait_x)
                    for a in range(QUAD):
                        rows = slice(32 * a, 32 * a + 32)
                        nc.vector.tensor_copy(
                            ay[rows, buf].rearrange("p n r (s a j) -> p n (r s) a j", s=2, a=QUAD)[:, :, :, a, :],
                            t_part[rows, :, 0:2, :].rearrange("p n r (s j) -> p n (r s) j", s=2)).then_inc(mats_ready, 1)
                    for b in range(B):
                        rows = slice(64 * b, 64 * b + 64)
                        nc.vector.tensor_copy(ax[rows, buf, :, 64 * b:64 * b + 64],
                                              t_part[rows, :, 2, :]).then_inc(mats_ready, 1)

            def statistics(t, pair, i, part, first=False):
                if part == 0:
                    dve.wait_ge(loaded[i], 16 * B // BODY * (t - i) + 16 * B)
                    if not first:
                        dve.wait_ge(stat_summed, pair - 1)
                v = i % 4
                for g in range(GROUPS):
                    nc.vector.bn_stats(stats[:, v, GROUPS * part + g, :],
                                       xin[:, i, part, QG * g:QG * (g + 1), :].rearrange("p q f -> p (q f)")
                                       ).then_inc(bn_done, 1)
                if part == B - 1:
                    dve.wait_ge(bn_done, B * GROUPS * (t + 1))
                    nc.vector.tensor_tensor(stats[:, v, :, 0:6:3], stats[:, v, :, 1:6:3], stats[:, v, :, 1:6:3],
                                            ALU.mult).then_inc(stats_ready, 1)

            def low_part(t, k):
                dve.wait_ge(y_hi_ready, POS * t + k + 1)
                nc.vector.tensor_tensor(y_lo[:, k].rearrange("p q r m -> p (q r m)"),
                                        yp[k][:].rearrange("p q m -> p (q m)"),
                                        y_hi[:, k].rearrange("p q r m -> p (q r m)"),
                                        ALU.subtract).then_inc(y_lo_ready, 1)

            def add_x(t, i, k):
                dve.wait_ge(x_done, POS * t + k + 1)
                nc.vector.tensor_tensor(result[:, i % SLOTS, :, 2 * k:2 * k + 2, :].rearrange("p b q f -> p b (q f)"),
                                        xp[k][:].rearrange("p b q r w -> p b (q r w)"),
                                        xin[:, i, :, 2 * k:2 * k + 2, :].rearrange("p b q f -> p b (q f)"),
                                        ALU.add).then_inc(result_ready, 1)

            for part in range(4):
                matrices(0, 0, part, None)
            for i in range(4):
                for b in range(B):
                    statistics(i, i // 2, i, b, first=True)

            def step(t0, pair, i, c, buf, head, lead, end):
                t = t0 + i
                start = head and i == 0
                more = not (end and i >= BODY - 4)
                if more:
                    statistics(t + 4, pair + 2, (i + 4) % BODY, 0)
                if not start:
                    add_x(t - 1, (i - 1) % BODY, 1)
                low_part(t, 0)
                if more:
                    statistics(t + 4, pair + 2, (i + 4) % BODY, 1)
                low_part(t, 1)
                if not start:
                    add_x(t - 1, (i - 1) % BODY, 2)
                low_part(t, 2)
                if not (head and i < SLOTS):
                    dve.wait_ge(stored[i % SLOTS], 16 * B // SLOTS * (t - i % SLOTS))
                add_x(t, i, 0)
                if lead and i >= 4 and not (isinstance(c, int) and c == NSUPER - 1):
                    matrices(c + 1, 1 - buf, i - 4, None if head else POS * STEPS * c)
            run(dve, step)
            for k in (1, 2):
                add_x(NSUPER * STEPS - 1, BODY - 1, k)

        @block.scalar
        def _(act):
            act.wait_ge(taps_sq, 1)
            nc.scalar.activation(tap_sq[:], tap[:], ACT.Square).then_inc(taps_sq, 1)
            act.wait_ge(taps_sq, 2)
            nc.scalar.activation(tap_e[:], tap_sq[:], ACT.Exp, scale=-2.0).then_inc(taps_exp, 1)

            def squares(c):
                act.wait_ge(dist_ready, 2 * c + 2)
                nc.scalar.activation(t_isq[:], t_int[:], ACT.Square).then_inc(sq_ready, 1)
                nc.scalar.activation(t_fsq[:], t_full[:], ACT.Square).then_inc(sq_ready, 1)
                act.wait_ge(sq_ready, 2 * c + 2)
                nc.scalar.activation(t_exp[:], t_fsq[:], ACT.Exp, scale=-2.0).then_inc(exp_ready, 1)

            def sum_parts(pair, v):
                cols = 3 * 2 * B * GROUPS
                act.wait_ge(stat_summed, pair + 1)
                nc.scalar.activation(parts[:, v, 0], sp_[:, 2:cols:3], ACT.Copy, bias=EPS,
                                     scale=2.0 / (QG * ROW)).then_inc(parts_ready, 1)
                nc.scalar.activation(parts[:, v, 1], sp_[:, 0:cols:3], ACT.Copy).then_inc(parts_ready, 1)
                nc.scalar.activation(parts[:, v, 2], sp_[:, 1:cols:3], ACT.Square).then_inc(parts_ready, 1)
                nc.scalar.activation(parts[:, v, 3], sp_[:, 1:cols:3], ACT.Copy, scale=-1.0).then_inc(parts_ready, 1)

            def normalise(t, pair, i, g, first):
                if g == 0:
                    act.wait_ge(coef_ready, pair + 1)
                    if not first:
                        act.wait_ge(lo_ready, GROUPS * (t - 1))
                v = i % 2
                for b in range(B):
                    col = B * GROUPS * (i % 2) + GROUPS * b + g
                    nc.scalar.activation(norm[:, v, 2 * QG * g:2 * QG * (g + 1), b, :],
                                         xin[:, i, b, QG * g:QG * (g + 1), :].rearrange("p q (r w) -> p (q r) w", r=2),
                                         ACT.Identity, bias=bias[:, i // 2 % 2, col:col + 1],
                                         scale=rstd[:, i // 2 % 2, col:col + 1]).then_inc(norm_ready, 1)

            def high_norm(t, i, g, first):
                act.wait_ge(norm_ready, B * GROUPS * t + B * (g + 1))
                if g == 0 and not first:
                    act.wait_ge(y_done, POS * (t - 1))
                v = i % 2
                cols = slice(2 * QG * g, 2 * QG * (g + 1))
                nc.scalar.activation(norm_hi[:, v, cols].rearrange("p q b w -> p (q b w)"),
                                     norm[:, v, cols].rearrange("p q b w -> p (q b w)"),
                                     ACT.Copy).then_inc(hi_ready, 1)

            def high_part(t, k, first):
                act.wait_ge(y_done, POS * t + k + 1)
                if not first:
                    act.wait_ge(x_done, POS * (t - 1) + k + 1)
                nc.scalar.activation(y_hi[:, k].rearrange("p q r m -> p (q r m)"),
                                     yp[k][:].rearrange("p q m -> p (q m)"), ACT.Copy).then_inc(y_hi_ready, 1)

            squares(0)
            sum_parts(0, 0)
            for g in range(GROUPS):
                normalise(0, 0, 0, g, True)
            for g in range(GROUPS):
                high_norm(0, 0, g, True)

            def step(t0, pair, i, c, buf, head, lead, end):
                t = t0 + i
                start = head and i == 0
                more = not (end and i == BODY - 1)
                if more:
                    normalise(t + 1, pair + i % 2, (i + 1) % BODY, 0, start)
                    high_norm(t + 1, (i + 1) % BODY, 0, start)
                high_part(t, 0, start)
                if i % 2 == 0 and not (end and i == BODY - 2):
                    sum_parts(pair + 1, (i // 2 + 1) % 2)
                if more:
                    normalise(t + 1, pair + i % 2, (i + 1) % BODY, 1, start)
                    high_norm(t + 1, (i + 1) % BODY, 1, start)
                high_part(t, 1, start)
                high_part(t, 2, start)
                if lead and i == 2 and not (isinstance(c, int) and c == NSUPER - 1):
                    squares(c + 1)
            run(act, step)

        @block.tensor
        def _(pe):
            def products(dst, pairs):
                for m, (w, mov) in enumerate(pairs):
                    last = nc.tensor.matmul(dst, w, mov, start=(m == 0), stop=(m == len(pairs) - 1))
                return last

            def sum_stats(pair, v, first=False):
                pe.wait_ge(stats_ready, 2 * (pair + 1))
                if not first:
                    pe.wait_ge(parts_ready, 4 * pair)
                for half in range(2):
                    last = nc.tensor.matmul(sp_[:, 0:3 * 2 * B * GROUPS], ones[:, :],
                                            stats[:, 2 * v:2 * v + 2, :, 3 * half:3 * half + 3]
                                            .rearrange("p t g s -> p (t g) s"),
                                            start=(half == 0), stop=(half == 1))
                last.then_inc(stat_summed, 1)

            def y_product(t, i, k, buf, first):
                if k < 2:
                    pe.wait_ge(lo_ready, GROUPS * t + k + 1)
                if not first:
                    pe.wait_ge(y_lo_ready, POS * (t - 1) + k + 1)
                v = i % 2
                for q in range(2):
                    pairs = []
                    for r in range(2):
                        hi, lo = (o[:, v, 2 * (2 * k + q) + r].rearrange("p b w -> p (b w)") for o in (norm_hi, norm_lo))
                        pairs += [(hi, ay_hi[:, buf, k, r]), (hi, ay_lo[:, buf, k, r]), (lo, ay_hi[:, buf, k, r])]
                    last = products(yp[k][:, q], pairs)
                last.then_inc(y_done, 1)

            def x_product(t, k, buf, first):
                pe.wait_ge(y_lo_ready, POS * t + k + 1)
                if not first:
                    pe.wait_ge(result_ready, POS * (t - 1) + k + 1)
                for q in range(2):
                    for r in range(2):
                        hi, lo = y_hi[:, k, q, r], y_lo[:, k, q, r]
                        last = products(xp[k][:, :, q, r, :], [(hi, ax_hi[:, buf, k]), (hi, ax_lo[:, buf, k]),
                                                               (lo, ax_hi[:, buf, k])])
                last.then_inc(x_done, 1)

            pe.wait_ge(consts, CONSTS)
            sum_stats(0, 0, first=True)

            def step(t0, pair, i, c, buf, head, lead, end):
                t = t0 + i
                start = head and i == 0
                buf_before = 1 - buf if lead and i == 0 else buf
                if lead and i == 0:
                    pe.wait_ge(mats_ready, MATS * (c + 1))
                y_product(t, i, 0, buf, start)
                if not start:
                    x_product(t - 1, 1, buf_before, head and i == 1)
                if i % 2 == 0 and not (end and i == BODY - 2):
                    sum_stats(pair + 1, (i // 2 + 1) % 2)
                y_product(t, i, 1, buf, start)
                if not start:
                    x_product(t - 1, 2, buf_before, head and i == 1)
                y_product(t, i, 2, buf, start)
                x_product(t, 0, buf, start)
            run(pe, step)
            for k in (1, 2):
                x_product(NSUPER * STEPS - 1, k, 1, False)


_INS = ["x", "L0_conv_offset"]


def kernel(**inputs):
    import numpy as _np
    import concourse.bacc as _bacc
    from concourse import mybir as _mybir
    from concourse.bass_utils import run_bass_kernel_spmd as _run

    nc = _bacc.Bacc("TRN2", target_bir_lowering=False, num_devices=1)
    arrays, args = {}, []
    for name in _INS:
        a = _np.ascontiguousarray(inputs[name])
        arrays[f"in_{name}_dram"] = a
        args.append(nc.dram_tensor(f"in_{name}_dram", a.shape, _mybir.dt.from_np(a.dtype), kind="ExternalInput").ap())
    args.append(nc.dram_tensor("out_dram", (BATCH, CH, HW, HW), F32, kind="ExternalOutput").ap())
    displaced_conv(nc, *args)
    r = _run(nc, [arrays], core_ids=[0])
    return r.results[0]["out_dram"]
```

```python
import concourse.bass as bass
from concourse import mybir
from contextlib import ExitStack

F32 = mybir.dt.float32
F16 = mybir.dt.float16
I32 = mybir.dt.int32
ALU = mybir.AluOpType
ACT = mybir.ActivationFunctionType
AX = mybir.AxisListType

BATCH, CH, HW = 32, 384, 64
P = 128
POSITIONS = 48
QUAD = 4
SUPER = 24
NSUPER = CH // SUPER
Q = SUPER // QUAD
POS = 3
GROUPS = 2
QG = Q // GROUPS
B = 2
STEPS = BATCH // B
BODY = 8
SLOTS = 4
LAG = 2
ROW = 2 * HW
COLS = Q * 2 * B * HW
HALF = COLS // GROUPS
EPS = 1e-5
TAPS = 5
ROUND = 12582912.0
FAR = 200.0
WINDOWS = [(0, 10), (0, 18), (0, 26), (0, 32), (6, 26), (14, 18), (22, 10)]
ALL_ROWS = WINDOWS[3]


def displaced_conv(nc: bass.Bass, x: bass.AP, offset: bass.AP, out: bass.AP):
    def tiled(a):
        return (a.rearrange("n c h w -> n (c h w)")
                 .rearrange("(m i b) (s q p f) -> m i b s p q f", i=BODY, b=B, s=NSUPER, q=Q, p=P))

    x_t, out_t = tiled(x), tiled(out)
    off_row = offset.rearrange("(o p) k -> o (p k)", o=1)

    with ExitStack() as ctx:
        def sb(name, shape, dt=F32):
            return ctx.enter_context(nc.sbuf_tensor(name, shape, dt))

        def sem(name):
            return ctx.enter_context(nc.semaphore(name))

        xin = sb("xin", [P, BODY, B, Q, ROW])
        norm = sb("norm", [P, 2, Q * 2, B, HW])
        norm_hi = sb("norm_hi", [P, 2, Q * 2, B, HW], F16)
        norm_lo = sb("norm_lo", [P, 2, Q * 2, B, HW], F16)
        y = sb("y", [P, POS, 2, 2, P])
        result = sb("result", [P, SLOTS, B, Q, ROW])
        stats = sb("stats", [P, 4, B * GROUPS, 6])
        sums = sb("sums", [P, 2, 2 * B * GROUPS, 6])
        both = sb("both", [P, 2, 2 * B * GROUPS, 3])
        mean_sq = sb("mean_sq", [P, 2, 2 * B * GROUPS])
        minus_mean = sb("minus_mean", [P, 2, 2 * B * GROUPS])
        mhalf = sb("mhalf", [P, 2 * B * GROUPS])
        spread = sb("spread", [P, 2, 2 * B * GROUPS])
        var = sb("var", [P, 2, 2 * B * GROUPS])
        rstd = sb("rstd", [P, 2, 2 * B * GROUPS])
        bias = sb("bias", [P, 2, 2 * B * GROUPS])
        ones = sb("ones", [P, P])
        zeros = sb("zeros", [P, 4 * P], F16)
        ay_hi = sb("ay_hi", [P, 2, POS, 2, 2 * P], F16)
        ay_lo = sb("ay_lo", [P, 2, POS, 2, 2 * P], F16)
        ax = sb("ax", [P, 2, POS, P])
        grid_i = sb("grid_i", [P, 3, HW], I32)
        grid = sb("grid", [P, 3, HW])
        src_i = sb("src_i", [P, 3], I32)
        src = sb("src", [P, 3])
        off = sb("off", [P, POSITIONS, 2])
        offc = sb("offc", [P, POSITIONS, 2])
        rnd_a = sb("rnd_a", [P, POSITIONS, 2])
        rnd = sb("rnd", [P, POSITIONS, 2])
        sub = sb("sub", [P, POSITIONS, 2])
        tap = sb("tap", [P, TAPS, POSITIONS * 2])
        tap_sq = sb("tap_sq", [P, TAPS, POSITIONS * 2])
        tap_e = sb("tap_e", [P, TAPS, POSITIONS * 2])
        tap_sum = sb("tap_sum", [P, POSITIONS, 2])
        tap_inv = sb("tap_inv", [P, POSITIONS, 2])
        shift3 = sb("shift3", [P, POSITIONS, 3])
        sub3 = sb("sub3", [P, POSITIONS, 3])
        inv3 = sb("inv3", [P, POSITIONS, 3])
        place3 = sb("place3", [P, POSITIONS, 3])
        ok_lo = sb("ok_lo", [P, POSITIONS, 3])
        ok_hi = sb("ok_hi", [P, POSITIONS, 3])
        valid3 = sb("valid3", [P, POSITIONS, 3])
        gain3 = sb("gain3", [P, POSITIONS, 3])
        dy_max = sb("dy_max", [P, NSUPER])
        dy_min = sb("dy_min", [P, NSUPER])
        window = sb("window", [P, 2 * len(WINDOWS) + 1, NSUPER])
        window_i = sb("window_i", [P, NSUPER], I32)
        t_int = sb("t_int", [P, POS, 3, HW])
        t_full = sb("t_full", [P, POS, 3, HW])
        t_isq = sb("t_isq", [P, POS, 3, HW])
        t_fsq = sb("t_fsq", [P, POS, 3, HW])
        t_exp = sb("t_exp", [P, POS, 3, HW])
        t_msk = sb("t_msk", [P, POS, 3, HW])
        t_val = sb("t_val", [P, POS, 3, HW])
        t_hi = sb("t_hi", [P, POS, 2, HW], F16)
        t_lo = sb("t_lo", [P, POS, 2, HW], F16)

        yp = [ctx.enter_context(nc.psum_tensor(f"yp{k}", [P, 2, 2 * P], F32)) for k in range(POS)]
        xp = [ctx.enter_context(nc.psum_tensor(f"xp{k}", [P, B, 2, 2, HW], F32)) for k in range(POS)]
        sp_ = ctx.enter_context(nc.psum_tensor("sp_", [P, 512], F32))

        loaded = [sem(f"loaded{i}") for i in range(BODY)]
        stored = [sem(f"stored{i}") for i in range(SLOTS)]
        off_loaded = sem("off_loaded")
        bn_done = sem("bn_done")
        stats_ready = sem("stats_ready")
        stat_summed = sem("stat_summed")
        sums_ready = sem("sums_ready")
        small = sem("small")
        rstd_ready = sem("rstd_ready")
        coef_ready = sem("coef_ready")
        norm0_ready = sem("norm0_ready")
        norm1_ready = sem("norm1_ready")
        hi_ready = sem("hi_ready")
        lo_ready = sem("lo_ready")
        y_done = sem("y_done")
        y_ready = sem("y_ready")
        x_done = sem("x_done")
        result_ready = sem("result_ready")
        consts = sem("consts")
        filled = sem("filled")
        shifts = sem("shifts")
        prep = sem("prep")
        taps_sq = sem("taps_sq")
        taps_exp = sem("taps_exp")
        classes = sem("classes")
        dist_ready = sem("dist_ready")
        sq_ready = sem("sq_ready")
        exp_ready = sem("exp_ready")
        made = sem("made")
        t_hi_ready = sem("t_hi_ready")
        t_lo_ready = sem("t_lo_ready")
        mats_ready = sem("mats_ready")

        block = ctx.enter_context(nc.Block())

        def run(eng, step):
            def superblock(c, buf, head=False, tail=False):
                for m in range(STEPS // BODY):
                    for i in range(BODY):
                        step(STEPS * c + BODY * m, STEPS // 2 * c + (BODY * m + i) // 2, i, c, buf,
                             head and m == 0, BODY * m + i, tail and m == STEPS // BODY - 1)
            superblock(0, 0, head=True)
            with eng.Fori(0, NSUPER // 2 - 1) as n:
                superblock(2 * n + 1, 1)
                superblock(2 * n + 2, 0)
            superblock(NSUPER - 1, 1, tail=True)

        @block.sync
        def _(sync):
            sync.dma_start(off[:, :, :], off_row.to_broadcast([P, 2 * POSITIONS])).then_inc(off_loaded, 16)

            def load(m, i, c):
                for b in range(B):
                    sync.dma_start(xin[:, i, b], x_t[m, i, b, c]).then_inc(loaded[i], 16)

            def store(m, i, c):
                for b in range(B):
                    sync.dma_start(out_t[m, i, b, c], result[:, i % SLOTS, b]).then_inc(stored[i % SLOTS], 16)

            def body(c, m, c_next, m_next):
                for i in range(BODY):
                    sync.wait_ge(result_ready, POS * (STEPS * c + BODY * m + i + 2))
                    store(m, i, c)
                    if m_next is not None:
                        load(m_next, i, c_next)

            for i in range(BODY):
                load(0, i, 0)
            with sync.Fori(0, NSUPER - 1) as c:
                body(c, 0, c, 1)
                body(c, 1, c + 1, 0)
            body(NSUPER - 1, 0, NSUPER - 1, 1)
            body(NSUPER - 1, 1, None, None)
            for i in range(SLOTS):
                sync.wait_ge(stored[i], 16 * B * NSUPER * STEPS // SLOTS)

        SMALLS = 5
        MADES = 2
        MATS = 2 * QUAD + B
        IOTAS = 2 * QUAD + 2 * B
        FILLS = 6

        def ay_block(m, t_part, buf, a):
            rows = slice(32 * a, 32 * a + 32)
            return (m[rows, buf].rearrange("p n r (s a j) -> p n (r s) a j", s=2, a=QUAD)[:, :, :, a, :],
                    t_part[rows].rearrange("p n r (s j) -> p n (r s) j", s=2))

        @block.gpsimd
        def _(pool):
            for a in range(QUAD):
                rows = slice(32 * a, 32 * a + 32)
                pool.iota(grid_i[rows, 0:2, :], pattern=[[1, 2], [-1, 2], [-2, 32]], base=0,
                          channel_multiplier=2).then_inc(consts, 1)
                pool.iota(src_i[rows, 0:2], pattern=[[1, 2]], base=0, channel_multiplier=2).then_inc(consts, 1)
            pool.wait_ge(consts, 2 * QUAD)
            for b in range(B):
                rows = slice(64 * b, 64 * b + 64)
                pool.iota(grid_i[rows, 2:3, :], pattern=[[0, 1], [-1, HW]], base=0,
                          channel_multiplier=1).then_inc(consts, 1)
                pool.iota(src_i[rows, 2:3], pattern=[[0, 1]], base=0, channel_multiplier=1).then_inc(consts, 1)
            pool.wait_ge(consts, IOTAS)
            pool.memset(ones[:, :], 1.0 / (2 * P)).then_inc(filled, 1)
            pool.memset(mhalf[:, :], -0.5).then_inc(filled, 1)
            pool.memset(ax[:], 0.0).then_inc(filled, 1)
            pool.memset(ay_lo[:], 0.0).then_inc(filled, 1)
            pool.memset(zeros[:, :], 0.0).then_inc(filled, 1)

            def distances(c):
                if c is 0:
                    pool.wait_ge(shifts, 1)
                else:
                    pool.wait_ge(mats_ready, MATS * c)
                at = bass.ds(POS * c, POS)
                pool.tensor_tensor(t_int[:], grid[:, None, :, :].to_broadcast([P, POS, 3, HW]),
                                   shift3[:, at, :].unsqueeze(3).to_broadcast([P, POS, 3, HW]),
                                   ALU.add).then_inc(dist_ready, 1)
                pool.wait_ge(dist_ready, 2 * c + 1)
                pool.tensor_tensor(t_full[:], t_int[:],
                                   sub3[:, at, :].unsqueeze(3).to_broadcast([P, POS, 3, HW]),
                                   ALU.add).then_inc(dist_ready, 1)

            def low_matrices(c):
                pool.wait_ge(t_hi_ready, c + 1)
                pool.tensor_tensor(t_lo[:], t_val[:, :, 0:2], t_hi[:], ALU.subtract).then_inc(t_lo_ready, 1)

            def coefficients(pair, v):
                pool.wait_ge(small, SMALLS * (pair + 1))
                pool.tensor_tensor(rstd[:, v], var[:, v], mhalf[:, :], ALU.pow).then_inc(rstd_ready, 1)
                pool.wait_ge(rstd_ready, pair + 1)
                pool.tensor_tensor(bias[:, v], minus_mean[:, v], rstd[:, v], ALU.mult).then_inc(coef_ready, 1)

            def low_part(t, v, g):
                pool.wait_ge(hi_ready, GROUPS * t + g + 1)
                cols = slice(2 * QG * g, 2 * QG * (g + 1))
                pool.tensor_tensor(norm_lo[:, v, cols], norm[:, v, cols], norm_hi[:, v, cols],
                                   ALU.subtract).then_inc(lo_ready, 1)

            distances(0)
            coefficients(0, 0)
            low_matrices(0)
            for g in range(GROUPS):
                low_part(0, 0, g)
            coefficients(1, 1)

            def step(t0, pair, i, c, buf, head, at, end):
                more = not (end and i == BODY - 1)
                for g in range(GROUPS):
                    if more:
                        low_part(t0 + i + 1, (i + 1) % 2, g)
                if i % 2 == 1 and not (end and i >= BODY - 3):
                    coefficients(pair + 2, i // 2 % 2)
                if not (isinstance(c, int) and c == NSUPER - 1):
                    if at == 1:
                        distances(c + 1)
                    if at == 6:
                        low_matrices(c + 1)
            run(pool, step)

        @block.vector
        def _(dve):
            n = [0]

            def own(ins):
                n[0] += 1
                ins.then_inc(prep, 1)

            def settle():
                dve.wait_ge(prep, n[0])

            def tsc(o, i, s1, s2, op0, op1):
                own(nc.vector.tensor_scalar(o, i, s1, s2, op0, op1))

            def shift_and_fraction():
                nc.vector.memset(ay_hi[:], 0.0).then_inc(filled, 1)
                dve.wait_ge(off_loaded, 16)
                tsc(offc[:], off[:], FAR, -FAR, ALU.min, ALU.max)
                settle()
                tsc(rnd_a[:], offc[:], ROUND, 0.0, ALU.add, ALU.add)
                settle()
                tsc(rnd[:], rnd_a[:], -ROUND, 0.0, ALU.add, ALU.add)
                dve.wait_ge(consts, IOTAS)
                own(nc.vector.tensor_copy(grid[:], grid_i[:]))
                own(nc.vector.tensor_copy(src[:], src_i[:]))
                settle()
                own(nc.vector.tensor_tensor(sub[:], offc[:], rnd[:], ALU.subtract))
                for kind in range(3):
                    own(nc.vector.tensor_copy(shift3[:, :, kind], rnd[:, :, 1 if kind < 2 else 0]))
                settle()
                for kind in range(3):
                    own(nc.vector.tensor_copy(sub3[:, :, kind], sub[:, :, 1 if kind < 2 else 0]))
                for k in range(TAPS):
                    tsc(tap[:, k, :], sub[:].rearrange("p n k -> p (n k)"), float(k - TAPS // 2), 0.0, ALU.add, ALU.add)
                settle()
                nc.vector.engine_nop().then_inc(shifts, 1)
                nc.vector.engine_nop().then_inc(taps_sq, 1)

            def all_gains():
                own(nc.vector.tensor_tensor(place3[:], shift3[:],
                                            src[:, None, :].to_broadcast([P, POSITIONS, 3]), ALU.add))
                settle()
                tsc(ok_lo[:], place3[:], 0.0, 0.0, ALU.is_ge, ALU.add)
                tsc(ok_hi[:], place3[:], float(HW - 1), 0.0, ALU.is_le, ALU.add)
                dve.wait_ge(taps_exp, 1)
                own(nc.vector.tensor_reduce(tap_sum[:].rearrange("p n k -> p (n k)"),
                                            tap_e[:].rearrange("p t m -> p m t"), AX.X, ALU.add))
                settle()
                own(nc.vector.reciprocal(tap_inv[:], tap_sum[:]))
                own(nc.vector.tensor_tensor(valid3[:], ok_lo[:], ok_hi[:], ALU.mult))
                settle()
                for kind in range(3):
                    own(nc.vector.tensor_copy(inv3[:, :, kind], tap_inv[:, :, 1 if kind < 2 else 0]))
                settle()
                own(nc.vector.tensor_tensor(gain3[:], valid3[:], inv3[:], ALU.mult))
                settle()

            def row_classes():
                dy = rnd[:, :, 1].rearrange("p (s k) -> p s k", k=POS)
                own(nc.vector.tensor_reduce(dy_max[:], dy, AX.X, ALU.max))
                own(nc.vector.tensor_reduce(dy_min[:], dy, AX.X, ALU.min))
                own(nc.vector.memset(window[:, 0], 3.0))
                settle()
                cut = [(first, count) for first, count in WINDOWS if (first, count) != ALL_ROWS]
                for w, (first, count) in enumerate(cut):
                    if first == 0:
                        tsc(window[:, 2 * w + 1], dy_max[:], float(2 * count - HW - 2), 0.0, ALU.is_le, ALU.add)
                    else:
                        tsc(window[:, 2 * w + 1], dy_min[:], float(2 * first + 2), 0.0, ALU.is_ge, ALU.add)
                settle()
                for w, (first, count) in enumerate(cut):
                    own(nc.vector.tensor_tensor(window[:, 2 * w + 2], window[:, 2 * w], window[:, 2 * w + 1],
                                                ALU.subtract if first == 0 else ALU.add))
                    settle()
                nc.vector.tensor_copy(window_i[:], window[:, 2 * len(cut)]).then_inc(classes, 1)

            def values(c):
                dve.wait_ge(exp_ready, c + 1)
                nc.vector.scalar_tensor_tensor(out=t_msk[:].rearrange("p a k w -> p (a k w)"),
                                               in0=t_isq[:].rearrange("p a k w -> p (a k w)"), scalar=4.0,
                                               in1=t_exp[:].rearrange("p a k w -> p (a k w)"),
                                               op0=ALU.is_le, op1=ALU.mult).then_inc(made, 1)
                dve.wait_ge(made, MADES * c + 1)
                nc.vector.tensor_tensor(t_val[:], t_msk[:],
                                        gain3[:, bass.ds(POS * c, POS), :].unsqueeze(3).to_broadcast([P, POS, 3, HW]),
                                        ALU.mult).then_inc(made, 1)

            def fill_low(c, buf, wait_x):
                if wait_x is not None:
                    dve.wait_ge(x_done, wait_x)
                dve.wait_ge(t_lo_ready, c + 1)
                for a in range(QUAD):
                    to, part = ay_block(ay_lo, t_lo, buf, a)
                    nc.vector.tensor_copy(to, part).then_inc(mats_ready, 1)

            def statistics(t, pair, i, part, first=False):
                if part == 0:
                    dve.wait_ge(loaded[i], 16 * B // BODY * (t - i) + 16 * B)
                    if not first:
                        dve.wait_ge(stat_summed, pair - 1)
                v = i % 4
                for g in range(GROUPS):
                    nc.vector.bn_stats(stats[:, v, GROUPS * part + g, :],
                                       xin[:, i, part, QG * g:QG * (g + 1), :].rearrange("p q f -> p (q f)")
                                       ).then_inc(bn_done, 1)
                if part == B - 1:
                    dve.wait_ge(bn_done, B * GROUPS * (t + 1))
                    nc.vector.tensor_tensor(stats[:, v, :, 0:6:3], stats[:, v, :, 1:6:3], stats[:, v, :, 1:6:3],
                                            ALU.mult).then_inc(stats_ready, 1)

            def variance(pair, v, part):
                mean = both[:, v, :, 1]
                if part == 0:
                    dve.wait_ge(sums_ready, pair + 1)
                    nc.vector.tensor_tensor(both[:, v], sums[:, v, :, 0:3], sums[:, v, :, 3:6],
                                            ALU.add).then_inc(small, 1)
                if part == 1:
                    dve.wait_ge(small, SMALLS * pair + 1)
                    nc.vector.tensor_scalar(minus_mean[:, v], mean, -1.0, 0.0, ALU.mult, ALU.add).then_inc(small, 1)
                    nc.vector.tensor_tensor(mean_sq[:, v], mean, mean, ALU.mult).then_inc(small, 1)
                    nc.vector.scalar_tensor_tensor(out=spread[:, v], in0=both[:, v, :, 2], scalar=2.0 / (QG * ROW),
                                                   in1=both[:, v, :, 0], op0=ALU.mult, op1=ALU.add).then_inc(small, 1)
                if part == 2:
                    dve.wait_ge(small, SMALLS * pair + 4)
                    nc.vector.scalar_tensor_tensor(out=var[:, v], in0=spread[:, v], scalar=EPS, in1=mean_sq[:, v],
                                                   op0=ALU.add, op1=ALU.subtract).then_inc(small, 1)

            def normalise(t, pair, i, first=False):
                dve.wait_ge(coef_ready, pair + 1)
                if not first:
                    dve.wait_ge(lo_ready, GROUPS * (t - 1))
                for b in range(B):
                    col = B * GROUPS * (i % 2) + GROUPS * b + 1
                    nc.vector.tensor_scalar(norm[:, i % 2, 2 * QG:, b, :],
                                            xin[:, i, b, QG:, :].rearrange("p q (r w) -> p (q r) w", r=2),
                                            rstd[:, i // 2 % 2, col:col + 1], bias[:, i // 2 % 2, col:col + 1],
                                            ALU.mult, ALU.add).then_inc(norm1_ready, 1)

            def add_x(t, i, k):
                dve.wait_ge(x_done, POS * t + k + 1)
                nc.vector.tensor_tensor(result[:, i % SLOTS, :, 2 * k:2 * k + 2, :].rearrange("p b q f -> p b (q f)"),
                                        xp[k][:].rearrange("p b q r w -> p b (q r w)"),
                                        xin[:, i, :, 2 * k:2 * k + 2, :].rearrange("p b q f -> p b (q f)"),
                                        ALU.add).then_inc(result_ready, 1)

            shift_and_fraction()
            for i in range(2):
                for b in range(B):
                    statistics(i, 0, i, b, first=True)
            for part in range(3):
                variance(0, 0, part)
            all_gains()
            values(0)
            dve.wait_ge(filled, FILLS)
            fill_low(0, 0, None)
            normalise(0, 0, 0, first=True)
            for i in range(2, 4):
                for b in range(B):
                    statistics(i, 1, i, b, first=True)
            for b in range(B):
                statistics(4, 2, 4, b)
            row_classes()
            for part in range(3):
                variance(1, 1, part)
            nc.vector.engine_nop().then_inc(result_ready, POS)

            def step(t0, pair, i, c, buf, head, at, end):
                t = t0 + i
                start = head and i == 0
                more = not (end and i >= BODY - 5)
                coefs = i % 2 == 1 and not (end and i >= BODY - 3)

                if not (end and i == BODY - 1):
                    normalise(t + 1, pair + i % 2, (i + 1) % BODY, start)
                if more:
                    statistics(t + 5, pair + 2 + i % 2, (i + 5) % BODY, 0)
                if not start:
                    add_x(t - 1, (i - 1) % BODY, 1)
                if more:
                    statistics(t + 5, pair + 2 + i % 2, (i + 5) % BODY, 1)
                if coefs:
                    variance(pair + 2, i // 2 % 2, 0)
                if not start:
                    add_x(t - 1, (i - 1) % BODY, 2)
                if coefs:
                    variance(pair + 2, i // 2 % 2, 1)
                if not (head and i < SLOTS):
                    dve.wait_ge(stored[i % SLOTS], 16 * B // SLOTS * (t - i % SLOTS))
                add_x(t, i, 0)
                if coefs:
                    variance(pair + 2, i // 2 % 2, 2)
                if end and i == BODY - 5:
                    nc.vector.engine_nop().then_inc(stats_ready, 4)
                if at == 4 and not (isinstance(c, int) and c == NSUPER - 1):
                    values(c + 1)
                if at == 8 and not (isinstance(c, int) and c == NSUPER - 1):
                    fill_low(c + 1, 1 - buf, None if c is 0 else POS * STEPS * c)
            run(dve, step)
            for k in (1, 2):
                add_x(NSUPER * STEPS - 1, BODY - 1, k)

        @block.scalar
        def _(act):
            act.wait_ge(taps_sq, 1)
            nc.scalar.activation(tap_sq[:], tap[:], ACT.Square).then_inc(taps_sq, 1)
            act.wait_ge(taps_sq, 2)
            nc.scalar.activation(tap_e[:], tap_sq[:], ACT.Exp, scale=-2.0).then_inc(taps_exp, 1)

            def squares(c):
                act.wait_ge(dist_ready, 2 * c + 2)
                nc.scalar.activation(t_isq[:], t_int[:], ACT.Square).then_inc(sq_ready, 1)
                nc.scalar.activation(t_fsq[:], t_full[:], ACT.Square).then_inc(sq_ready, 1)
                act.wait_ge(sq_ready, 2 * c + 2)
                nc.scalar.activation(t_exp[:], t_fsq[:], ACT.Exp, scale=-2.0).then_inc(exp_ready, 1)

            def high_matrices(c):
                act.wait_ge(made, MADES * (c + 1))
                nc.scalar.activation(t_hi[:], t_val[:, :, 0:2], ACT.Copy).then_inc(t_hi_ready, 1)

            def fill(c, buf, part, wait_x):
                if part == 0:
                    if wait_x is not None:
                        act.wait_ge(x_done, wait_x)
                    act.wait_ge(t_hi_ready, c + 1)
                if part < QUAD:
                    to, t_part = ay_block(ay_hi, t_hi, buf, part)
                    nc.scalar.activation(to, t_part, ACT.Copy).then_inc(mats_ready, 1)
                else:
                    b = part - QUAD
                    rows = slice(64 * b, 64 * b + 64)
                    nc.scalar.activation(ax[rows, buf, :, 64 * b:64 * b + 64], t_val[rows, :, 2, :],
                                         ACT.Copy).then_inc(mats_ready, 1)

            def copy_sums(pair, v):
                act.wait_ge(stat_summed, pair + 1)
                nc.scalar.activation(sums[:, v].rearrange("p g s -> p (g s)"), sp_[:, 0:6 * 2 * B * GROUPS],
                                     ACT.Copy).then_inc(sums_ready, 1)

            def normalise(t, pair, i, first):
                act.wait_ge(coef_ready, pair + 1)
                if not first:
                    act.wait_ge(lo_ready, GROUPS * (t - 1))
                for b in range(B):
                    col = B * GROUPS * (i % 2) + GROUPS * b
                    nc.scalar.activation(norm[:, i % 2, 0:2 * QG, b, :],
                                         xin[:, i, b, 0:QG, :].rearrange("p q (r w) -> p (q r) w", r=2),
                                         ACT.Identity, bias=bias[:, i // 2 % 2, col:col + 1],
                                         scale=rstd[:, i // 2 % 2, col:col + 1]).then_inc(norm0_ready, 1)

            def high_norm(t, i, g, first):
                act.wait_ge((norm0_ready, norm1_ready)[g], B * (t + 1))
                if g == 0 and not first:
                    act.wait_ge(y_done, POS * (t - 1))
                v = i % 2
                cols = slice(2 * QG * g, 2 * QG * (g + 1))
                nc.scalar.activation(norm_hi[:, v, cols].rearrange("p q b w -> p (q b w)"),
                                     norm[:, v, cols].rearrange("p q b w -> p (q b w)"),
                                     ACT.Copy).then_inc(hi_ready, 1)

            def copy_y(t, k, first):
                act.wait_ge(y_done, POS * t + k + 1)
                if not first:
                    act.wait_ge(x_done, POS * (t - 1) + k + 1)
                nc.scalar.activation(y[:, k].rearrange("p q r m -> p (q r m)"),
                                     yp[k][:].rearrange("p q m -> p (q m)"), ACT.Copy).then_inc(y_ready, 1)

            copy_sums(0, 0)
            squares(0)
            high_matrices(0)
            act.wait_ge(filled, FILLS)
            for part in range(QUAD + B):
                fill(0, 0, part, None)
            normalise(0, 0, 0, True)
            for g in range(GROUPS):
                high_norm(0, 0, g, True)
            copy_sums(1, 1)

            def step(t0, pair, i, c, buf, head, at, end):
                t = t0 + i
                start = head and i == 0
                more = not (end and i == BODY - 1)
                if more:
                    normalise(t + 1, pair + i % 2, (i + 1) % BODY, start)
                    high_norm(t + 1, (i + 1) % BODY, 0, start)
                copy_y(t, 0, start)
                if i % 2 == 1:
                    copy_sums(pair + 2, i // 2 % 2)
                if more:
                    high_norm(t + 1, (i + 1) % BODY, 1, start)
                copy_y(t, 1, start)
                copy_y(t, 2, start)
                if not (isinstance(c, int) and c == NSUPER - 1):
                    if at == 2:
                        squares(c + 1)
                    if at == 5:
                        high_matrices(c + 1)
                    if 6 <= at < 6 + QUAD + B:
                        fill(c + 1, 1 - buf, at - 6, None if c is 0 else POS * STEPS * c)
            run(act, step)

        @block.tensor
        def _(pe):
            def products(dst, pairs):
                for m, (w, mov) in enumerate(pairs):
                    last = nc.tensor.matmul(dst, w, mov, start=(m == 0), stop=(m == len(pairs) - 1))
                return last

            def sum_stats(pair, v, first=False):
                pe.wait_ge(stats_ready, 2 * (pair + 1))
                if not first:
                    pe.wait_ge(sums_ready, pair)
                nc.tensor.matmul(sp_[:, 0:6 * 2 * B * GROUPS], ones[:, :],
                                 stats[:, 2 * v:2 * v + 2].rearrange("p t g s -> p (t g s)"),
                                 start=True, stop=True).then_inc(stat_summed, 1)

            def y_product(t, v, k, buf, rows, wait_bank=True, clear=False):
                if k < 2:
                    pe.wait_ge(lo_ready, GROUPS * t + k + 1)
                if wait_bank:
                    pe.wait_ge(y_ready, POS * (t - 1) + k + 1)
                if clear:
                    nc.tensor.matmul(yp[k][:].rearrange("p q m -> p (q m)"), zeros[:, :P], zeros[:, :],
                                     start=True, stop=True)
                cols = slice(rows[0], rows[0] + rows[1])
                for q in range(2):
                    pairs = []
                    for r in range(2):
                        hi, lo = (o[:, v, 2 * (2 * k + q) + r].rearrange("p b w -> p (b w)") for o in (norm_hi, norm_lo))
                        mov_hi, mov_lo = (m[:, buf, k, r].rearrange("p (ra j) -> p ra j", j=HW // 2)[:, :, cols]
                                          for m in (ay_hi, ay_lo))
                        pairs += [(hi, mov_hi), (hi, mov_lo), (lo, mov_hi)]
                    last = products(yp[k][:, q].rearrange("p (ra j) -> p ra j", j=HW // 2)[:, :, cols], pairs)
                last.then_inc(y_done, 1)

            def x_product(t, k, buf):
                pe.wait_ge(y_ready, POS * t + k + 1)
                pe.wait_ge(result_ready, POS * t + k + 1)
                for q in range(2):
                    for r in range(2):
                        last = products(xp[k][:, :, q, r, :], [(y[:, k, q, r], ax[:, buf, k])])
                last.then_inc(x_done, 1)

            pe.wait_ge(filled, FILLS)
            sum_stats(0, 0, first=True)
            sum_stats(1, 1)

            def step(t, pair, i, buf, rows, clear=False, first=False):
                buf_before = 1 - buf if i == 0 else buf
                y_product(t, i % 2, 0, buf, rows, not first, clear)
                if not first:
                    x_product(t - 1, 1, buf_before)
                if i % 2 == 1:
                    sum_stats(pair + 2, i // 2 % 2)
                y_product(t, i % 2, 1, buf, rows, not first, clear)
                if not first:
                    x_product(t - 1, 2, buf_before)
                y_product(t, i % 2, 2, buf, rows, not first, clear)
                x_product(t, 0, buf)

            def row_class(c):
                return pe.value_load(window_i[0:1, bass.ds(c, 1)], min_val=0, max_val=len(WINDOWS) - 1)

            def superblock(c, buf, cls, begin=0, lo=0, hi=len(WINDOWS)):
                if hi - lo > 1:
                    mid = (lo + hi) // 2
                    with pe.If(cls < mid):
                        superblock(c, buf, cls, begin, lo, mid)
                    with pe.Else():
                        superblock(c, buf, cls, begin, mid, hi)
                    return
                rows = WINDOWS[lo]
                t, pair = STEPS * c, STEPS // 2 * c
                if begin == 0:
                    pe.wait_ge(mats_ready, MATS * (c + 1))
                for i in range(begin, 2):
                    step(t + i, pair, i, buf, rows, clear=i == begin)
                with pe.Fori(0, 3) as m:
                    for i in range(2, 6):
                        step(t + 4 * m + i, pair + 2 * m + i // 2, i, buf, rows)
                for i in (14, 15):
                    step(t + i, pair + i // 2, i, buf, rows)

            pe.wait_ge(mats_ready, MATS)
            step(0, 0, 0, 0, ALL_ROWS, first=True)
            pe.wait_ge(classes, 1)
            superblock(0, 0, row_class(0), begin=1)
            with pe.Fori(0, NSUPER // 2 - 1) as n:
                class_odd, class_even = row_class(2 * n + 1), row_class(2 * n + 2)
                superblock(2 * n + 1, 1, class_odd)
                superblock(2 * n + 2, 0, class_even)
            superblock(NSUPER - 1, 1, row_class(NSUPER - 1))
            for k in (1, 2):
                x_product(NSUPER * STEPS - 1, k, 1)


_INS = ["x", "L0_conv_offset"]


def kernel(**inputs):
    import numpy as _np
    import concourse.bacc as _bacc
    from concourse import mybir as _mybir
    from concourse.bass_utils import run_bass_kernel_spmd as _run

    nc = _bacc.Bacc("TRN2", target_bir_lowering=False, num_devices=1)
    arrays, args = {}, []
    for name in _INS:
        a = _np.ascontiguousarray(inputs[name])
        arrays[f"in_{name}_dram"] = a
        args.append(nc.dram_tensor(f"in_{name}_dram", a.shape, _mybir.dt.from_np(a.dtype), kind="ExternalInput").ap())
    args.append(nc.dram_tensor("out_dram", (BATCH, CH, HW, HW), F32, kind="ExternalOutput").ap())
    displaced_conv(nc, *args)
    r = _run(nc, [arrays], core_ids=[0])
    return r.results[0]["out_dram"]
```
